# Optimizing a Trainium2 kernel written in Bass

```python
import numpy as np
import jax
import jax.numpy as jnp

def _softmax(x, axis=-1):
    return jax.nn.softmax(x, axis=axis)

def _gelu(x):
    return jax.nn.gelu(x, approximate=True)

def _silu(x):
    return jax.nn.silu(x)

def _sigmoid(x):
    return jax.nn.sigmoid(x)

def _layernorm(x, axis=-1, eps=1e-05):
    m = jnp.mean(x, axis=axis, keepdims=True)
    v = jnp.var(x, axis=axis, keepdims=True)
    return (x - m) / jnp.sqrt(v + eps)

def _scatter_add(tgt, idx, src, axis=0):
    return tgt.at[idx].add(src)

def _segment_sum(src, seg, n):
    return jax.ops.segment_sum(src, seg, n)
kernel_name = 'mk_rec_standalone_d1_rec_r8_303928'

def setup_inputs(seed: int=0):
    np.random.seed(seed)
    _w = jnp.asarray

    def _rec_inputs():
        import jax
        import jax.numpy as jnp
        _rk = jax.random.key(seed)
        r_inputs = -0.000154849 + 1.00019 * jax.random.normal(jax.random.fold_in(_rk, 1), (512, 40, 64), jnp.float32)
        return r_inputs
    r_inputs = _rec_inputs()

    def _L0_rec_setup():
        import jax, jax.numpy as jnp
        import numpy as np
        FIELD_NUM = 40
        EMBED_DIM = 64
        BATCH = 256
        _I, _J = np.triu_indices(FIELD_NUM, k=1)
        PAIR_I = jnp.asarray(_I)
        PAIR_J = jnp.asarray(_J)
        key = jax.random.key(seed)
        k1, k2 = jax.random.split(key)
        inputs = jax.random.normal(k1, (BATCH, FIELD_NUM, EMBED_DIM), dtype=jnp.float32)
        w = jax.random.normal(k2, (EMBED_DIM, EMBED_DIM), dtype=jnp.float32) * (1.0 / EMBED_DIM) ** 0.5
        return {'inputs': inputs, 'w': w}
    _L0_rec_all = _L0_rec_setup()
    _L0_rec_in = {k: v for k, v in _L0_rec_all.items() if k in ('w',)}
    del _L0_rec_all
    return {'r_inputs': r_inputs, 'L0_rec_w': _L0_rec_in['w']}

def reference(r_inputs, L0_rec_w):
    import jax
    import jax.numpy as jnp

    def _L0_rec_ref(inputs, w):
        import jax, jax.numpy as jnp
        import numpy as np
        FIELD_NUM = 40
        EMBED_DIM = 64
        BATCH = 256
        _I, _J = np.triu_indices(FIELD_NUM, k=1)
        PAIR_I = jnp.asarray(_I)
        PAIR_J = jnp.asarray(_J)
        xw = jnp.einsum('bfd,de->bfe', inputs, w)
        p = xw[:, PAIR_I, :] * inputs[:, PAIR_J, :]
        B = inputs.shape[0]
        return p.reshape(B, -1)
    y = _L0_rec_ref(r_inputs, L0_rec_w)
    return y

_drawn_inputs = setup_inputs


def setup_inputs(seed=0):
    import zlib

    import numpy as np

    out = dict(_drawn_inputs(seed))
    spreads = {}
    factors = {}
    for name, (base, spread) in spreads.items():
        noise = np.random.default_rng([zlib.crc32(name.encode()), seed]).standard_normal(out[name].shape)
        drawn = base * np.exp(spread * noise) if base else spread * noise
        out[name] = jnp.asarray(drawn.astype(out[name].dtype))
    for name, factor in factors.items():
        out[name] = (out[name] * factor).astype(out[name].dtype)
    return out
```

```python
from contextlib import ExitStack

import concourse.bass as bass
from concourse import mybir

F32 = mybir.dt.float32
ALU = mybir.AluOpType

P = 128
BANK = 512
PAIR = 2
GROUP = 4
HIGH_GROUPS = 2
DMA_DONE = 16
HALVES = 2
SLOTS = 8
CHUNK_FIRST = [32, 29, 26, 23, 20, 18, 16, 14, 12, 10, 8, 6, 4, 2, 1, 0]


def rec_pair_products(nc: bass.Bass, x: bass.AP, w: bass.AP, out: bass.AP):
    batch, fields, dim = x.shape
    tiles = batch // P
    groups = fields // GROUP
    row = fields * dim
    rounds = tiles // HALVES
    assert batch == rounds * HALVES * P and fields == groups * GROUP and PAIR * dim == P

    def pair_start(i):
        return i * (fields - 1) - i * (i - 1) // 2

    chunk_end = [fields - 1] + CHUNK_FIRST[:-1]
    chunks = list(zip(CHUNK_FIRST, chunk_end))
    chunk_pairs = [pair_start(end) - pair_start(first) for first, end in chunks]
    slot_pairs = max(chunk_pairs)
    uses = len(chunks) // SLOTS
    assert len(chunks) == uses * SLOTS and CHUNK_FIRST[-1] == 0

    x_rows = x.rearrange("b f d -> b (f d)")
    high = (groups - HIGH_GROUPS) * GROUP * dim

    with ExitStack() as ctx:
        def sbuf(name, shape):
            return ctx.enter_context(nc.sbuf_tensor(name, shape, F32))

        def psum(name, shape):
            return ctx.enter_context(nc.psum_tensor(name, shape, F32))

        def sem(name):
            return ctx.enter_context(nc.semaphore(name))

        ident = sbuf("ident", [P, P])
        w_twice = sbuf("w_twice", [P, dim])
        x_sb = sbuf("x_sb", [P, HALVES, row])
        xw_sb = sbuf("xw_sb", [P, HALVES, row])
        xT_sb = sbuf("xT_sb", [P, 2, GROUP // PAIR, P])
        products = sbuf("products", [P, SLOTS, slot_pairs * dim])
        xT_ps = [psum(f"xT_ps{n}", [P, GROUP // PAIR, P]) for n in range(2)]
        xw_ps = [psum(f"xw_ps{n}", [P, PAIR, BANK]) for n in range(2)]

        ident_zeroed = sem("ident_zeroed")
        ident_ready = sem("ident_ready")
        w_landed = [sem("w_landed0"), sem("w_landed1")]
        x_high_landed = [sem(f"x_high_landed{h}") for h in range(HALVES)]
        x_low_landed = [sem(f"x_low_landed{h}") for h in range(HALVES)]
        turned = sem("turned")
        turned_copied = sem("turned_copied")
        projected = sem("projected")
        xw_ready = sem("xw_ready")
        chunk_ready = sem("chunk_ready")
        slot_free = [sem(f"slot_free{s}") for s in range(SLOTS)]

        block = ctx.enter_context(nc.Block())

        def load_x_high(eng, t, half):
            eng.dma_start(x_sb[:, half, high:row],
                          x_rows[bass.ds(t * P, P), high:row]).then_inc(x_high_landed[half], DMA_DONE)

        def load_x_low(eng, t, half):
            eng.dma_start(x_sb[:, half, 0:high],
                          x_rows[bass.ds(t * P, P), 0:high]).then_inc(x_low_landed[half], DMA_DONE)

        @block.sync
        def _(sp):
            def store_tile(t):
                for c, (first, end) in enumerate(chunks):
                    slot = c % SLOTS
                    sp.wait_ge(chunk_ready, t * len(chunks) + (c + 1))
                    sp.nop(nofuse=True)
                    sp.dma_start(out[bass.ds(t * P, P), pair_start(first) * dim:pair_start(end) * dim],
                                 products[:, slot, 0:chunk_pairs[c] * dim]).then_inc(slot_free[slot], DMA_DONE)

            for h, landed in enumerate(w_landed):
                sp.dma_start(w_twice[h * dim:(h + 1) * dim, :], w).then_inc(landed, DMA_DONE)
            load_x_low(sp, 0, 0)
            load_x_high(sp, 1, 1)
            load_x_low(sp, 1, 1)
            with sp.Fori(0, rounds - 1) as r:
                for half in range(HALVES):
                    store_tile(r * HALVES + half)
                    load_x_high(sp, r * HALVES + (half + HALVES), half)
                    load_x_low(sp, r * HALVES + (half + HALVES), half)
            with sp.Fori(tiles - HALVES, tiles) as t:
                store_tile(t)
            for slot in range(SLOTS):
                sp.wait_ge(slot_free[slot], DMA_DONE * (uses * tiles + 1))

        @block.gpsimd
        def _(pool):
            nc.gpsimd.memset(ident[:, :], 0.0).then_inc(ident_zeroed, 1)
            pool.wait_ge(ident_zeroed, 1)
            nc.gpsimd.affine_select(out=ident[:, :], in_=ident[:, :], compare_op=ALU.not_equal, fill=1.0, base=0,
                                    pattern=[[-1, P]], channel_multiplier=1).then_inc(ident_ready, 1)

        @block.tensor
        def _(pe):
            def turn(half, n):
                g = groups - 1 - n
                for k in range(GROUP // PAIR):
                    at = (g * GROUP + k * PAIR) * dim
                    last = nc.tensor.transpose(xT_ps[n % 2][:, k, :], x_sb[:, half, at:at + P], ident[:, :])
                last.then_inc(turned, 1)

            def project(t, n):
                pe.wait_ge(turned_copied, t * groups + (n + 1))
                for f in range(GROUP):
                    pair, side = divmod(f, PAIR)
                    d_rows = slice(side * dim, (side + 1) * dim)
                    last = nc.tensor.matmul(xw_ps[n % 2][:, side, pair * dim:(pair + 1) * dim],
                                            xT_sb[d_rows, n % 2, pair, :], w_twice[d_rows, :], start=True, stop=True)
                last.then_inc(projected, 1)

            pe.wait_ge(ident_ready, 1)
            for landed in w_landed:
                pe.wait_ge(landed, DMA_DONE)
            with pe.Fori(0, rounds) as r:
                for half in range(HALVES):
                    t = r * HALVES + half
                    pe.wait_ge(x_high_landed[half], r * DMA_DONE + DMA_DONE)
                    for n in range(HIGH_GROUPS):
                        turn(half, n)
                    for n in range(HIGH_GROUPS):
                        project(t, n)
                    pe.wait_ge(x_low_landed[half], r * DMA_DONE + DMA_DONE)
                    turn(half, HIGH_GROUPS)
                    for n in range(HIGH_GROUPS, groups):
                        if n + 1 < groups:
                            turn(half, n + 1)
                        project(t, n)

        @block.scalar
        def _(act):
            def copy_turned(t, n):
                act.wait_ge(turned, t * groups + (n + 1))
                nc.scalar.copy(xT_sb[:, n % 2, :, :], xT_ps[n % 2][:, :, :]).then_inc(turned_copied, 1)

            def copy_projected(t, half, n):
                g = groups - 1 - n
                act.wait_ge(projected, t * groups + (n + 1))
                nc.scalar.copy(
                    xw_sb[:, half, g * GROUP * dim:(g + 1) * GROUP * dim].rearrange(
                        "p (pair side e) -> p side pair e", side=PAIR, e=dim),
                    xw_ps[n % 2][:, :, 0:GROUP // PAIR * dim].rearrange(
                        "p side (pair e) -> p side pair e", e=dim)).then_inc(xw_ready, 1)

            load_x_high(act, 0, 0)
            with act.Fori(0, rounds) as r:
                for half in range(HALVES):
                    t = r * HALVES + half
                    for n in range(HIGH_GROUPS):
                        copy_turned(t, n)
                    for n in range(HIGH_GROUPS):
                        copy_projected(t, half, n)
                    copy_turned(t, HIGH_GROUPS)
                    for n in range(HIGH_GROUPS, groups):
                        if n + 1 < groups:
                            copy_turned(t, n + 1)
                        copy_projected(t, half, n)

        @block.vector
        def _(dve):
            for slot in range(SLOTS):
                dve.sem_inc(slot_free[slot], DMA_DONE)
            with dve.Fori(0, rounds) as r:
                for half in range(HALVES):
                    t = r * HALVES + half
                    for c, (first, end) in enumerate(chunks):
                        slot = c % SLOTS
                        dve.wait_ge(slot_free[slot], t * (DMA_DONE * uses) + DMA_DONE * (c // SLOTS + 1))
                        for i in reversed(range(first, end)):
                            if i == fields - 2 or i % GROUP == GROUP - 1:
                                dve.wait_ge(xw_ready, t * groups + (groups - i // GROUP))
                            later = fields - 1 - i
                            at = (pair_start(i) - pair_start(first)) * dim
                            last = nc.vector.tensor_tensor(
                                products[:, slot, at:at + later * dim].rearrange("p (j e) -> p j e", e=dim),
                                xw_sb[:, half, i * dim:(i + 1) * dim].unsqueeze(1).to_broadcast([P, later, dim]),
                                x_sb[:, half, (i + 1) * dim:row].rearrange("p (j e) -> p j e", e=dim), ALU.mult)
                        last.then_inc(chunk_ready, 1)


def kernel(r_inputs, L0_rec_w):
    import numpy as np
    import concourse.bacc as bacc
    from concourse.bass_utils import run_bass_kernel_spmd

    batch, fields, dim = r_inputs.shape
    arrays = {
        "x_dram": np.ascontiguousarray(r_inputs),
        "w_dram": np.ascontiguousarray(L0_rec_w),
    }
    nc = bacc.Bacc("TRN2", target_bir_lowering=False, num_devices=1)
    ins = [nc.dram_tensor(name, a.shape, F32, kind="ExternalInput").ap() for name, a in arrays.items()]
    out_shape = (batch, fields * (fields - 1) // 2 * dim)
    out = nc.dram_tensor("out_dram", out_shape, F32, kind="ExternalOutput").ap()
    rec_pair_products(nc, *ins, out)
    return run_bass_kernel_spmd(nc, [arrays], core_ids=[0]).results[0]["out_dram"]
```

```python
from contextlib import ExitStack

import concourse.bass as bass
from concourse import mybir

F32 = mybir.dt.float32
ALU = mybir.AluOpType

P = 128
BANK = 512
PAIR = 2
GROUP = 4
HIGH_GROUPS = 2
DMA_DONE = 16
HALVES = 2
SLOTS = 8
CHUNK_FIRST = [32, 29, 26, 23, 20, 17, 14, 12, 10, 8, 6, 4, 3, 2, 1, 0]


def rec_pair_products(nc: bass.Bass, x: bass.AP, w: bass.AP, out: bass.AP):
    batch, fields, dim = x.shape
    tiles = batch // P
    groups = fields // GROUP
    row = fields * dim
    rounds = tiles // HALVES
    assert batch == rounds * HALVES * P and fields == groups * GROUP and PAIR * dim == P

    def pair_start(i):
        return i * (fields - 1) - i * (i - 1) // 2

    chunk_end = [fields - 1] + CHUNK_FIRST[:-1]
    chunks = list(zip(CHUNK_FIRST, chunk_end))
    chunk_pairs = [pair_start(end) - pair_start(first) for first, end in chunks]
    slot_pairs = max(chunk_pairs)
    uses = len(chunks) // SLOTS
    assert len(chunks) == uses * SLOTS and CHUNK_FIRST[-1] == 0

    x_rows = x.rearrange("b f d -> b (f d)")
    high = (groups - HIGH_GROUPS) * GROUP * dim

    with ExitStack() as ctx:
        def sbuf(name, shape):
            return ctx.enter_context(nc.sbuf_tensor(name, shape, F32))

        def psum(name, shape):
            return ctx.enter_context(nc.psum_tensor(name, shape, F32))

        def sem(name):
            return ctx.enter_context(nc.semaphore(name))

        ident = sbuf("ident", [P, P])
        w_twice = sbuf("w_twice", [P, dim])
        x_sb = sbuf("x_sb", [P, HALVES, row])
        x_early = sbuf("x_early", [P, (tiles - HALVES) * row])
        xw_sb = sbuf("xw_sb", [P, HALVES, row])
        xT_sb = sbuf("xT_sb", [P, 2, GROUP // PAIR, P])
        products = sbuf("products", [P, SLOTS, slot_pairs * dim])
        xT_ps = [psum(f"xT_ps{n}", [P, GROUP // PAIR, P]) for n in range(2)]
        xw_ps = [psum(f"xw_ps{n}", [P, PAIR, BANK]) for n in range(2)]

        ident_zeroed = sem("ident_zeroed")
        ident_ready = sem("ident_ready")
        w_landed = [sem("w_landed0"), sem("w_landed1")]
        x_high_ready = [sem(f"x_high_ready{h}") for h in range(HALVES)]
        x_low_ready = [sem(f"x_low_ready{h}") for h in range(HALVES)]
        x_early_landed = sem("x_early_landed")
        turned = sem("turned")
        turned_copied = sem("turned_copied")
        projected = sem("projected")
        xw_ready = sem("xw_ready")
        chunk_ready = sem("chunk_ready")
        slot_free = [sem(f"slot_free{s}") for s in range(SLOTS)]

        block = ctx.enter_context(nc.Block())

        def load_x_high(eng, t):
            eng.dma_start(x_sb[:, t, high:row], x_rows[t * P:(t + 1) * P, high:row]).then_inc(x_high_ready[t], DMA_DONE)

        def load_x_low(eng, t):
            eng.dma_start(x_sb[:, t, 0:high], x_rows[t * P:(t + 1) * P, 0:high]).then_inc(x_low_ready[t], DMA_DONE)

        @block.sync
        def _(sp):
            for h, landed in enumerate(w_landed):
                sp.dma_start(w_twice[h * dim:(h + 1) * dim, :], w).then_inc(landed, DMA_DONE)
            load_x_low(sp, 0)
            for t in range(1, HALVES):
                load_x_high(sp, t)
                load_x_low(sp, t)
            sp.dma_start(x_early.rearrange("p (t c) -> p t c", c=row),
                         x_rows[HALVES * P:batch, :].rearrange("(t p) c -> p t c", p=P)).then_inc(x_early_landed, DMA_DONE)
            with sp.Fori(0, tiles) as t:
                for c, (first, end) in enumerate(chunks):
                    slot = c % SLOTS
                    sp.wait_ge(chunk_ready, t * len(chunks) + (c + 1))
                    sp.nop(nofuse=True)
                    sp.dma_start(out[bass.ds(t * P, P), pair_start(first) * dim:pair_start(end) * dim],
                                 products[:, slot, 0:chunk_pairs[c] * dim]).then_inc(slot_free[slot], DMA_DONE)
            for slot in range(SLOTS):
                sp.wait_ge(slot_free[slot], DMA_DONE * (uses * tiles + 1))

        @block.gpsimd
        def _(pool):
            nc.gpsimd.memset(ident[:, :], 0.0).then_inc(ident_zeroed, 1)
            pool.wait_ge(ident_zeroed, 1)
            nc.gpsimd.affine_select(out=ident[:, :], in_=ident[:, :], compare_op=ALU.not_equal, fill=1.0, base=0,
                                    pattern=[[-1, P]], channel_multiplier=1).then_inc(ident_ready, 1)

        @block.tensor
        def _(pe):
            def turn(half, n):
                g = groups - 1 - n
                for k in range(GROUP // PAIR):
                    at = (g * GROUP + k * PAIR) * dim
                    last = nc.tensor.transpose(xT_ps[n % 2][:, k, :], x_sb[:, half, at:at + P], ident[:, :])
                last.then_inc(turned, 1)

            def project(t, n):
                pe.wait_ge(turned_copied, t * groups + (n + 1))
                for f in range(GROUP):
                    pair, side = divmod(f, PAIR)
                    d_rows = slice(side * dim, (side + 1) * dim)
                    last = nc.tensor.matmul(xw_ps[n % 2][:, side, pair * dim:(pair + 1) * dim],
                                            xT_sb[d_rows, n % 2, pair, :], w_twice[d_rows, :], start=True, stop=True)
                last.then_inc(projected, 1)

            pe.wait_ge(ident_ready, 1)
            for landed in w_landed:
                pe.wait_ge(landed, DMA_DONE)
            with pe.Fori(0, rounds) as r:
                for half in range(HALVES):
                    t = r * HALVES + half
                    pe.wait_ge(x_high_ready[half], r * DMA_DONE + DMA_DONE)
                    for n in range(HIGH_GROUPS):
                        turn(half, n)
                    for n in range(HIGH_GROUPS):
                        project(t, n)
                    pe.wait_ge(x_low_ready[half], r * DMA_DONE + DMA_DONE)
                    turn(half, HIGH_GROUPS)
                    for n in range(HIGH_GROUPS, groups):
                        if n + 1 < groups:
                            turn(half, n + 1)
                        project(t, n)

        @block.scalar
        def _(act):
            def copy_turned(t, n):
                act.wait_ge(turned, t * groups + (n + 1))
                nc.scalar.copy(xT_sb[:, n % 2, :, :], xT_ps[n % 2][:, :, :]).then_inc(turned_copied, 1)

            def copy_projected(t, half, n):
                g = groups - 1 - n
                act.wait_ge(projected, t * groups + (n + 1))
                nc.scalar.copy(
                    xw_sb[:, half, g * GROUP * dim:(g + 1) * GROUP * dim].rearrange(
                        "p (pair side e) -> p side pair e", side=PAIR, e=dim),
                    xw_ps[n % 2][:, :, 0:GROUP // PAIR * dim].rearrange(
                        "p side (pair e) -> p side pair e", e=dim)).then_inc(xw_ready, 1)

            def move_early(t, half):
                act.wait_ge(chunk_ready, (t - (HALVES - 1)) * len(chunks))
                at = (t - HALVES) * row
                nc.scalar.copy(x_sb[:, half, high:row],
                               x_early[:, bass.ds(at + high, row - high)]).then_inc(x_high_ready[half], DMA_DONE)
                nc.scalar.copy(x_sb[:, half, 0:high],
                               x_early[:, bass.ds(at, high)]).then_inc(x_low_ready[half], DMA_DONE)

            def copy_tile(t, half):
                for n in range(HIGH_GROUPS):
                    copy_turned(t, n)
                for n in range(HIGH_GROUPS):
                    copy_projected(t, half, n)
                copy_turned(t, HIGH_GROUPS)
                for n in range(HIGH_GROUPS, groups):
                    if n + 1 < groups:
                        copy_turned(t, n + 1)
                    copy_projected(t, half, n)

            load_x_high(act, 0)
            for half in range(HALVES):
                copy_tile(half, half)
            act.wait_ge(x_early_landed, DMA_DONE)
            with act.Fori(1, rounds) as r:
                for half in range(HALVES):
                    t = r * HALVES + half
                    move_early(t, half)
                    copy_tile(t, half)

        @block.vector
        def _(dve):
            for slot in range(SLOTS):
                dve.sem_inc(slot_free[slot], DMA_DONE)
            with dve.Fori(0, rounds) as r:
                for half in range(HALVES):
                    t = r * HALVES + half
                    for c, (first, end) in enumerate(chunks):
                        slot = c % SLOTS
                        dve.wait_ge(slot_free[slot], t * (DMA_DONE * uses) + DMA_DONE * (c // SLOTS + 1))
                        for i in reversed(range(first, end)):
                            if i == fields - 2 or i % GROUP == GROUP - 1:
                                dve.wait_ge(xw_ready, t * groups + (groups - i // GROUP))
                            later = fields - 1 - i
                            at = (pair_start(i) - pair_start(first)) * dim
                            last = nc.vector.tensor_tensor(
                                products[:, slot, at:at + later * dim].rearrange("p (j e) -> p j e", e=dim),
                                xw_sb[:, half, i * dim:(i + 1) * dim].unsqueeze(1).to_broadcast([P, later, dim]),
                                x_sb[:, half, (i + 1) * dim:row].rearrange("p (j e) -> p j e", e=dim), ALU.mult)
                        last.then_inc(chunk_ready, 1)


def kernel(r_inputs, L0_rec_w):
    import numpy as np
    import concourse.bacc as bacc
    from concourse.bass_utils import run_bass_kernel_spmd

    batch, fields, dim = r_inputs.shape
    arrays = {
        "x_dram": np.ascontiguousarray(r_inputs),
        "w_dram": np.ascontiguousarray(L0_rec_w),
    }
    nc = bacc.Bacc("TRN2", target_bir_lowering=False, num_devices=1)
    ins = [nc.dram_tensor(name, a.shape, F32, kind="ExternalInput").ap() for name, a in arrays.items()]
    out_shape = (batch, fields * (fields - 1) // 2 * dim)
    out = nc.dram_tensor("out_dram", out_shape, F32, kind="ExternalOutput").ap()
    rec_pair_products(nc, *ins, out)
    return run_bass_kernel_spmd(nc, [arrays], core_ids=[0]).results[0]["out_dram"]
```
